# Optimizing a Trainium2 kernel written in Bass

```python
import numpy as np
import jax
import jax.numpy as jnp

def _softmax(x, axis=-1):
    return jax.nn.softmax(x, axis=axis)

def _gelu(x):
    return jax.nn.gelu(x, approximate=True)

def _silu(x):
    return jax.nn.silu(x)

def _sigmoid(x):
    return jax.nn.sigmoid(x)

def _layernorm(x, axis=-1, eps=1e-05):
    m = jnp.mean(x, axis=axis, keepdims=True)
    v = jnp.var(x, axis=axis, keepdims=True)
    return (x - m) / jnp.sqrt(v + eps)

def _scatter_add(tgt, idx, src, axis=0):
    return tgt.at[idx].add(src)

def _segment_sum(src, seg, n):
    return jax.ops.segment_sum(src, seg, n)
kernel_name = 'mk_perceiver_d1_seqx_r4_397151'

def setup_inputs(seed: int=0):
    np.random.seed(seed)
    _w = jnp.asarray

    def _rec_inputs():
        import jax
        import jax.numpy as jnp
        _rk = jax.random.key(seed)
        x = 7.22e-05 + 1 * jax.random.normal(jax.random.fold_in(_rk, 1), (1, 128, 512), jnp.float32)
        _lenS = 128 - jax.random.randint(jax.random.fold_in(_rk, 7), (1,), 0, max(1, 128 // 4) + 1, jnp.int32)
        _lenS2 = 12544 - jax.random.randint(jax.random.fold_in(_rk, 8), (1,), 0, max(1, 12544 // 4) + 1, jnp.int32)
        _ctx_512P = jax.random.normal(jax.random.fold_in(_rk, 11), (1, 16, 128), jnp.float32)
        _ctx_512c = jax.random.dirichlet(jax.random.fold_in(_rk, 511), 0.3 * jnp.ones((16,), jnp.float32), (1, 12544))
        _ctx_512t = jnp.einsum('bsk,bkd->bsd', _ctx_512c, _ctx_512P)
        _ctx_512t = _ctx_512t * jax.lax.rsqrt(jnp.mean(jnp.square(_ctx_512t)) + 1e-12) * 0.953939
        ctx_512 = -0.000514642 + 1.00011 * (_ctx_512t + 0.3 * jax.random.normal(jax.random.fold_in(_rk, 611), (1, 12544, 128), jnp.float32))
        return (x, ctx_512)
    x, ctx_512 = _rec_inputs()

    def _L0_xattn_setup():
        import jax, jax.numpy as jnp
        import numpy as np
        B, S, H, NH, L = (2, 512, 512, 16, 128)
        HD = H // NH
        key = jax.random.key(seed)
        k1, k2, k3, k4, k5 = jax.random.split(key, 5)
        scale = 0.02
        return {'q': jax.random.normal(k1, (B, S, H), dtype=jnp.float32), 'latent_kv': jax.random.normal(k2, (B, S, L), dtype=jnp.float32), 'Wq': jax.random.normal(k3, (H, H), dtype=jnp.float32) * scale, 'Wkv_expand': jax.random.normal(k4, (2 * H, L), dtype=jnp.float32) * scale, 'Wout': jax.random.normal(k5, (H, H), dtype=jnp.float32) * scale}
    _L0_xattn_all = _L0_xattn_setup()
    _L0_xattn_in = {k: v for k, v in _L0_xattn_all.items() if k in ('Wq', 'Wkv_expand', 'Wout')}
    del _L0_xattn_all

    def _L0_attn_setup():
        import jax, jax.numpy as jnp
        import numpy as np
        NH = 16
        key = jax.random.key(seed)
        ks = jax.random.split(key, 5)
        B, T, D = (2, 512, 512)
        scale = 0.02
        return {'x': jax.random.normal(ks[0], (B, T, D), dtype=jnp.float32), 'Wq': jax.random.normal(ks[1], (D, D), dtype=jnp.float32) * scale, 'Wk': jax.random.normal(ks[2], (D, D), dtype=jnp.float32) * scale, 'Wv': jax.random.normal(ks[3], (D, D), dtype=jnp.float32) * scale, 'Wo': jax.random.normal(ks[4], (D, D), dtype=jnp.float32) * scale}
    _L0_attn_all = _L0_attn_setup()
    _L0_attn_in = {k: v for k, v in _L0_attn_all.items() if k in ('Wq', 'Wk', 'Wv', 'Wo')}
    del _L0_attn_all

    def _L0_ffn_setup():
        import jax, jax.numpy as jnp
        import numpy as np
        TOP_K = 6
        CAP_FACTOR = 2

        def _moe_block(x2d, wg_router, w_gate, w_up, w_down, ws_gate, ws_up, ws_down):
            T, D = x2d.shape
            E = wg_router.shape[0]
            scores = jax.nn.softmax(x2d @ wg_router.T, axis=-1)
            topk_w, topk_idx = jax.lax.top_k(scores, TOP_K)
            topk_w = topk_w / (jnp.sum(topk_w, axis=-1, keepdims=True) + 1e-20)
            flat_idx = topk_idx.reshape(-1)
            oh = jax.nn.one_hot(flat_idx, E, dtype=jnp.int32)
            pos = jnp.cumsum(oh, axis=0) - 1
            pos_in_e = jnp.take_along_axis(pos, flat_idx[:, None], axis=1)[:, 0]
            C = CAP_FACTOR * (T * TOP_K // E)
            valid = pos_in_e < C
            safe_pos = jnp.where(valid, pos_in_e, 0)
            tok_id = jnp.repeat(jnp.arange(T), TOP_K)
            vmask = valid[:, None].astype(x2d.dtype)
            x_rep = x2d[tok_id] * vmask
            xe = jnp.zeros((E, C, D), x2d.dtype).at[flat_idx, safe_pos].add(x_rep)
            g = jnp.einsum('ecd,edf->ecf', xe, w_gate)
            u = jnp.einsum('ecd,edf->ecf', xe, w_up)
            ye = jnp.einsum('ecf,efd->ecd', jax.nn.silu(g) * u, w_down)
            y_tok = ye[flat_idx, safe_pos] * vmask
            y = jnp.sum(y_tok.reshape(T, TOP_K, D) * topk_w[..., None], axis=1)
            sh = jax.nn.silu(x2d @ ws_gate) * (x2d @ ws_up) @ ws_down
            return y + sh
        key = jax.random.key(seed)
        ks = jax.random.split(key, 9)
        B, S, D, F, E = (1, 512, 512, 352, 32)
        FS = F * 2
        s = 0.02
        return {'hidden_states': jax.random.normal(ks[0], (B, S, D), jnp.float32), 'wg_router': jax.random.normal(ks[1], (E, D), jnp.float32) * s, 'w_gate': jax.random.normal(ks[2], (E, D, F), jnp.float32) * s, 'w_up': jax.random.normal(ks[3], (E, D, F), jnp.float32) * s, 'w_down': jax.random.normal(ks[4], (E, F, D), jnp.float32) * s, 'ws_gate': jax.random.normal(ks[5], (D, FS), jnp.float32) * s, 'ws_up': jax.random.normal(ks[6], (D, FS), jnp.float32) * s, 'ws_down': jax.random.normal(ks[7], (FS, D), jnp.float32) * s}
    _L0_ffn_all = _L0_ffn_setup()
    _L0_ffn_in = {k: v for k, v in _L0_ffn_all.items() if k in ('wg_router', 'w_gate', 'w_up', 'w_down', 'ws_gate', 'ws_up', 'ws_down')}
    del _L0_ffn_all
    return {'x': x, 'ctx_512': ctx_512, 'L0_xattn_Wq': _L0_xattn_in['Wq'], 'L0_xattn_Wkv_expand': _L0_xattn_in['Wkv_expand'], 'L0_xattn_Wout': _L0_xattn_in['Wout'], 'L0_attn_Wq': _L0_attn_in['Wq'], 'L0_attn_Wk': _L0_attn_in['Wk'], 'L0_attn_Wv': _L0_attn_in['Wv'], 'L0_attn_Wo': _L0_attn_in['Wo'], 'L0_ffn_wg_router': _L0_ffn_in['wg_router'], 'L0_ffn_w_gate': _L0_ffn_in['w_gate'], 'L0_ffn_w_up': _L0_ffn_in['w_up'], 'L0_ffn_w_down': _L0_ffn_in['w_down'], 'L0_ffn_ws_gate': _L0_ffn_in['ws_gate'], 'L0_ffn_ws_up': _L0_ffn_in['ws_up'], 'L0_ffn_ws_down': _L0_ffn_in['ws_down']}

def reference(x, ctx_512, L0_xattn_Wq, L0_xattn_Wkv_expand, L0_xattn_Wout, L0_attn_Wq, L0_attn_Wk, L0_attn_Wv, L0_attn_Wo, L0_ffn_wg_router, L0_ffn_w_gate, L0_ffn_w_up, L0_ffn_w_down, L0_ffn_ws_gate, L0_ffn_ws_up, L0_ffn_ws_down):
    import jax
    import jax.numpy as jnp

    def _L0_xattn_ref(q, latent_kv, Wq, Wkv_expand, Wout):
        import jax, jax.numpy as jnp
        import numpy as np
        B, S, H, NH, L = (2, 512, 512, 16, 128)
        HD = H // NH
        b, sq, _ = q.shape
        sk = latent_kv.shape[1]
        qp = q @ Wq.T
        kv = latent_kv @ Wkv_expand.T
        k, v = jnp.split(kv, 2, axis=-1)
        qh = qp.reshape(b, sq, NH, HD).transpose(0, 2, 1, 3)
        kh = k.reshape(b, sk, NH, HD).transpose(0, 2, 1, 3)
        vh = v.reshape(b, sk, NH, HD).transpose(0, 2, 1, 3)
        inv_sqrt_d = 1.0 / jnp.sqrt(jnp.float32(HD))
        scores = jnp.einsum('bhqd,bhkd->bhqk', qh, kh) * inv_sqrt_d
        causal = jnp.tril(jnp.ones((sq, sk), dtype=bool))
        scores = jnp.where(causal, scores, jnp.finfo(scores.dtype).min)
        attn = jax.nn.softmax(scores, axis=-1)
        out = jnp.einsum('bhqk,bhkd->bhqd', attn, vh)
        out = out.transpose(0, 2, 1, 3).reshape(b, sq, H)
        return out @ Wout.T

    def _L0_attn_ref(x, Wq, Wk, Wv, Wo):
        import jax, jax.numpy as jnp
        import numpy as np
        NH = 16
        B, T, D = x.shape
        hd = D // NH
        q = (x @ Wq.T).reshape(B, T, NH, hd).transpose(0, 2, 1, 3)
        k = (x @ Wk.T).reshape(B, T, NH, hd).transpose(0, 2, 1, 3)
        v = (x @ Wv.T).reshape(B, T, NH, hd).transpose(0, 2, 1, 3)
        att = jnp.einsum('bhtd,bhsd->bhts', q, k) / jnp.sqrt(jnp.asarray(hd, x.dtype))
        neg = jnp.finfo(att.dtype).min
        mask = jnp.triu(jnp.full((T, T), neg, dtype=att.dtype), k=1)
        att = att + mask
        w = jax.nn.softmax(att, axis=-1)
        z = jnp.einsum('bhts,bhsd->bhtd', w, v)
        z = z.transpose(0, 2, 1, 3).reshape(B, T, D)
        return z @ Wo.T

    def _L0_ffn_ref(hidden_states, wg_router, w_gate, w_up, w_down, ws_gate, ws_up, ws_down):
        import jax, jax.numpy as jnp
        import numpy as np
        TOP_K = 6
        CAP_FACTOR = 2

        def _moe_block(x2d, wg_router, w_gate, w_up, w_down, ws_gate, ws_up, ws_down):
            T, D = x2d.shape
            E = wg_router.shape[0]
            scores = jax.nn.softmax(x2d @ wg_router.T, axis=-1)
            topk_w, topk_idx = jax.lax.top_k(scores, TOP_K)
            topk_w = topk_w / (jnp.sum(topk_w, axis=-1, keepdims=True) + 1e-20)
            flat_idx = topk_idx.reshape(-1)
            oh = jax.nn.one_hot(flat_idx, E, dtype=jnp.int32)
            pos = jnp.cumsum(oh, axis=0) - 1
            pos_in_e = jnp.take_along_axis(pos, flat_idx[:, None], axis=1)[:, 0]
            C = CAP_FACTOR * (T * TOP_K // E)
            valid = pos_in_e < C
            safe_pos = jnp.where(valid, pos_in_e, 0)
            tok_id = jnp.repeat(jnp.arange(T), TOP_K)
            vmask = valid[:, None].astype(x2d.dtype)
            x_rep = x2d[tok_id] * vmask
            xe = jnp.zeros((E, C, D), x2d.dtype).at[flat_idx, safe_pos].add(x_rep)
            g = jnp.einsum('ecd,edf->ecf', xe, w_gate)
            u = jnp.einsum('ecd,edf->ecf', xe, w_up)
            ye = jnp.einsum('ecf,efd->ecd', jax.nn.silu(g) * u, w_down)
            y_tok = ye[flat_idx, safe_pos] * vmask
            y = jnp.sum(y_tok.reshape(T, TOP_K, D) * topk_w[..., None], axis=1)
            sh = jax.nn.silu(x2d @ ws_gate) * (x2d @ ws_up) @ ws_down
            return y + sh
        B, S, D = hidden_states.shape
        x2d = hidden_states.reshape(-1, D)
        out = _moe_block(x2d, wg_router, w_gate, w_up, w_down, ws_gate, ws_up, ws_down)
        return out.reshape(B, S, D)
    x = x + _L0_xattn_ref(_layernorm(x, axis=-1), ctx_512, L0_xattn_Wq, L0_xattn_Wkv_expand, L0_xattn_Wout)
    x = x + _L0_attn_ref(_layernorm(x, axis=-1), L0_attn_Wq, L0_attn_Wk, L0_attn_Wv, L0_attn_Wo)
    x = x + _L0_ffn_ref(_layernorm(x, axis=-1), L0_ffn_wg_router, L0_ffn_w_gate, L0_ffn_w_up, L0_ffn_w_down, L0_ffn_ws_gate, L0_ffn_ws_up, L0_ffn_ws_down)
    return x

_drawn_inputs = setup_inputs


def setup_inputs(seed=0):
    import zlib

    import numpy as np

    out = dict(_drawn_inputs(seed))
    spreads = {}
    factors = {'L0_xattn_Wq': 8.0, 'L0_attn_Wq': 6.191, 'L0_attn_Wk': 5.109, 'L0_ffn_wg_router': 2.815}
    for name, (base, spread) in spreads.items():
        noise = np.random.default_rng([zlib.crc32(name.encode()), seed]).standard_normal(out[name].shape)
        drawn = base * np.exp(spread * noise) if base else spread * noise
        out[name] = jnp.asarray(drawn.astype(out[name].dtype))
    for name, factor in factors.items():
        out[name] = (out[name] * factor).astype(out[name].dtype)
    return out
```

```python
from contextlib import ExitStack

import concourse.bass as bass
from concourse import mybir

F32 = mybir.dt.float32
ALU = mybir.AluOpType
ACT = mybir.ActivationFunctionType
AX_X = mybir.AxisListType.X

P = 128
D = 512
DC = D // P
NH = 16
HD = D // NH
HPC = P // HD
E = 32
TOP_K = 6
CAP = 2 * (P * TOP_K // E)
SLOTS = 64
F = 352
FT = F - 2 * P
PAIRS = E // 2
RING = 5
GATE = DC * 2 * F
UP0 = GATE
DOWN0 = 2 * GATE
TAIL0 = DOWN0 + 2 * 2 * D
SLOT = TAIL0 + 2 * D
XW = DC * D + 2 * D + DC * D
AW = 4 * DC * D
SCALE = 1.0 / float(HD) ** 0.5
EPS = 1e-5
MASKED = -3.4028234663852886e38
LN = 3


def perceiver_layer(nc, x_d, ctxT_d, xw_d, aw_d, wg_d, sh_d, sh_tail_d, pair_d, pair_tail_d, out_d):
    ctx = ExitStack()
    with ctx:
        def sb(name, shape):
            return ctx.enter_context(nc.sbuf_tensor(name, shape, F32))

        def sem(name):
            return ctx.enter_context(nc.semaphore(name))

        ring = sb("ring", [P, RING * SLOT])
        x = sb("x", [P, D])
        xn = sb("xn", [P, D])
        xnT = sb("xnT", [P, DC, P])
        ctxT = sb("ctxT", [P, P])
        wg = sb("wg", [P, DC, E])
        ident = sb("ident", [P, P])
        before = sb("before", [P, P])
        causal = sb("causal", [P, P])
        headmask = sb("headmask", [P, HPC])
        slot_no = sb("slot_no", [P, SLOTS])
        stats = sb("stats", [P, LN, 6])
        meanvar = sb("meanvar", [P, LN, 2])
        std = sb("std", [P, LN])
        rstd = sb("rstd", [P, LN])
        warm = sb("warm", [P, 2])
        nmax = sb("nmax", [P, 2 * DC, HPC])
        rowsum = sb("rowsum", [P, 2 * DC, HPC])
        rrow = sb("rrow", [P, 2 * DC, HPC])
        lmax = sb("lmax", [P, 1])
        lsum = sb("lsum", [P, 1])
        rlsum = sb("rlsum", [P, 1])
        lexp = sb("lexp", [P, E])
        score = sb("score", [P, E + 2])
        top = sb("top", [P, 8])
        rest = sb("rest", [P, E + 2])
        chosen = sb("chosen", [P, E])
        wsum = sb("wsum", [P, 1])
        rwsum = sb("rwsum", [P, 1])
        weight = sb("weight", [P, E])
        place = sb("place", [P, E])
        arena = sb("arena", [P, 5632])

        def part(at, n):
            return arena[:, at:at + n]

        qT = part(0, 512).rearrange("p (c t) -> p c t", c=DC)
        kx = part(512, 1024).rearrange("p (b h k) -> p b h k", b=2, h=HPC)
        prob = part(1536, 2048).rearrange("p (b h k) -> p b h k", b=DC, h=HPC)
        probT = part(3584, 1024).rearrange("p (b h q) -> p b h q", b=2, h=HPC)
        v = part(4608, 512)
        oT = part(5120, 512).rearrange("p (c t) -> p c t", c=DC)

        xeT = part(0, 512).rearrange("p (c s) -> p c s", c=DC)
        silu = part(512, 352)
        h = part(864, 352)
        hsT = part(1216, 512)
        ye = part(1728, 512)
        gather = part(2240, 128)
        scatter = part(2368, 128)
        final = part(2496, 512)

        bank = [ctx.enter_context(nc.psum_tensor(f"bank{i}", [P, 512], F32)) for i in range(8)]
        ps_z, ps_o, ps_t, ps_q, ps_k, ps_v = bank[0], bank[1], bank[4], bank[5], bank[6], bank[7]
        ps_s = [bank[2], bank[3]]
        ps_xT = [bank[4], bank[5]]
        ps_xe = [bank[2], bank[3]]
        ps_g, ps_u, ps_h, ps_ye, ps_y, ps_r = bank[4], bank[5], bank[6], bank[7], bank[0], bank[1]

        x_in = sem("x_in")
        kv_in = sem("kv_in")
        xq_in = sem("xq_in")
        xo_in = sem("xo_in")
        aw_in = [sem(f"aw{n}_in") for n in range(4)]
        wg_in = sem("wg_in")
        gate_in = [sem(f"gate_in{s}") for s in range(RING)]
        up_in = [sem(f"up_in{s}") for s in range(RING)]
        down_in = [sem(f"down_in{s}") for s in range(RING)]
        tail_in = [sem(f"tail_in{s}") for s in range(RING)]
        out_done = sem("out_done")
        const_base = sem("const_base")
        const_made = sem("const_made")
        warm_set = sem("warm_set")
        x_ready = sem("x_ready")
        stats_made = sem("stats_made")
        meanvar_made = sem("meanvar_made")
        eps_added = sem("eps_added")
        std_made = sem("std_made")
        rstd_made = sem("rstd_made")
        xn_ready = sem("xn_ready")
        xnT_psum = sem("xnT_psum")
        xnT_a = sem("xnT_a")
        xnT_b = sem("xnT_b")
        q_psum = sem("q_psum")
        q_ready = sem("q_ready")
        k_psum = sem("k_psum")
        k_ready = sem("k_ready")
        v_psum = sem("v_psum")
        v_ready = sem("v_ready")
        s_psum = sem("s_psum")
        s_masked = sem("s_masked")
        nmax_ready = sem("nmax_ready")
        exp_done = sem("exp_done")
        rrow_ready = sem("rrow_ready")
        prob_ready = sem("prob_ready")
        probT_psum = sem("probT_psum")
        probT_ready = sem("probT_ready")
        o_psum = sem("o_psum")
        o_ready = sem("o_ready")
        z_psum = sem("z_psum")
        logits = sem("logits")
        route = sem("route")
        lexp_ready = sem("lexp_ready")
        chosen_ready = sem("chosen_ready")
        count_psum = sem("count_psum")
        gate_psum = sem("gate_psum")
        up_psum = sem("up_psum")
        silu_ready = sem("silu_ready")
        h_ready = sem("h_ready")
        hT_psum = sem("hT_psum")
        hT_ready = sem("hT_ready")
        down_done = sem("down_done")
        gather_ready = sem("gather_ready")
        scatter_ready = sem("scatter_ready")
        xe_psum = sem("xe_psum")
        xe_a = sem("xe_a")
        xe_b = sem("xe_b")
        ye_ready = sem("ye_ready")
        y_psum = sem("y_psum")
        final_ready = sem("final_ready")

        def slot(s, at, n):
            return ring[:, s * SLOT + at:s * SLOT + at + n]

        def gate_w(s):
            return slot(s, 0, GATE).rearrange("p (c e f) -> p c e f", c=DC, e=2)

        def up_w(s):
            return slot(s, UP0, GATE).rearrange("p (c e f) -> p c e f", c=DC, e=2)

        def down_w(s):
            return slot(s, DOWN0, 4 * D).rearrange("p (c e n) -> p c e n", c=2, e=2)

        def tail_w(s):
            return ring[0:FT, s * SLOT + TAIL0:s * SLOT + SLOT].rearrange("p (e n) -> p e n", e=2)

        xq_w = slot(3, 0, DC * D).rearrange("p (c n) -> p c n", c=DC)
        kv_w = slot(3, DC * D, 2 * D)
        xo_w = slot(3, DC * D + 2 * D, DC * D).rearrange("p (c n) -> p c n", c=DC)
        a_w = [slot(4, n * DC * D, DC * D).rearrange("p (c n) -> p c n", c=DC) for n in range(4)]
        q_w, o_w = [xq_w, a_w[0]], [xo_w, a_w[3]]
        q_in, o_in = [xq_in, aw_in[0]], [xo_in, aw_in[3]]

        block = ctx.enter_context(nc.Block())

        @block.sync
        def _(sp):
            sp.dma_start(x[:, :], x_d).then_inc(x_in, 16)
            sp.dma_start(ctxT[:, :], ctxT_d).then_inc(kv_in, 16)
            sp.dma_start(kv_w, xw_d[:, DC * D:DC * D + 2 * D]).then_inc(kv_in, 16)
            sp.dma_start(slot(3, 0, DC * D), xw_d[:, 0:DC * D]).then_inc(xq_in, 16)
            sp.dma_start(slot(3, DC * D + 2 * D, DC * D), xw_d[:, DC * D + 2 * D:XW]).then_inc(xo_in, 16)
            for n in range(4):
                sp.dma_start(slot(4, n * DC * D, DC * D),
                             aw_d[:, n * DC * D:(n + 1) * DC * D]).then_inc(aw_in[n], 16)
            sp.dma_start(wg[:, :, :], wg_d.rearrange("p (c e) -> p c e", c=DC)).then_inc(wg_in, 16)

            def load_gate(s, src):
                sp.dma_start(slot(s, 0, GATE), src[:, 0:GATE]).then_inc(gate_in[s], 16)

            def load_up(s, src):
                sp.dma_start(slot(s, UP0, GATE), src[:, UP0:UP0 + GATE]).then_inc(up_in[s], 16)

            def load_down(s, src, tail):
                sp.dma_start(slot(s, DOWN0, 4 * D), src[:, DOWN0:TAIL0]).then_inc(down_in[s], 16)
                sp.dma_start(ring[0:FT, s * SLOT + TAIL0:s * SLOT + SLOT], tail).then_inc(tail_in[s], 16)

            load_gate(0, sh_d)
            load_up(0, sh_d)
            load_down(0, sh_d, sh_tail_d)
            for p in range(RING - 1):
                s = p + 1
                if s == 3:
                    sp.wait_ge(z_psum, 1)
                if s == 4:
                    sp.wait_ge(z_psum, 2)
                load_gate(s, pair_d[p])
                load_up(s, pair_d[p])
                load_down(s, pair_d[p], pair_tail_d[p])

            def load_pair(p, s):
                src = pair_d[bass.ds(p, 1)].rearrange("a p n -> (a p) n")
                tail = pair_tail_d[bass.ds(p, 1)].rearrange("a p n -> (a p) n")
                sp.wait_ge(gate_psum, p - 2)
                load_gate(s, src)
                sp.wait_ge(up_psum, p - 2)
                load_up(s, src)
                sp.wait_ge(down_done, p - 2)
                load_down(s, src, tail)

            with sp.Fori(0, 2) as i:
                for j in range(RING):
                    load_pair(i * RING + (RING - 1 + j), j)
            for p in range(3 * RING - 1, PAIRS):
                load_pair(p, (p + 1) % RING)

            sp.wait_ge(final_ready, 1)
            sp.dma_start(out_d, final).then_inc(out_done, 16)
            sp.wait_ge(out_done, 16)

        @block.gpsimd
        def _(pool):
            pool.memset(ident[:, :], 0.0).then_inc(const_base, 1)
            pool.memset(before[:, :], 1.0).then_inc(const_base, 1)
            pool.memset(causal[:, :], 0.0).then_inc(const_base, 1)
            pool.memset(headmask[:, :], 1.0).then_inc(const_base, 1)
            pool.iota(slot_no[:, :], pattern=[[1, SLOTS]], base=1, channel_multiplier=0,
                      allow_small_or_imprecise_dtypes=True).then_inc(const_base, 1)
            pool.memset(score[:, E:E + 1], -1.0).then_inc(const_base, 1)
            pool.memset(score[:, E + 1:E + 2], -2.0).then_inc(const_base, 1)
            pool.wait_ge(const_base, 7)
            pool.affine_select(out=ident[:, :], in_=ident[:, :], compare_op=ALU.not_equal, fill=1.0,
                               base=0, pattern=[[-1, P]], channel_multiplier=1).then_inc(const_made, 1)
            pool.affine_select(out=headmask[:, :], in_=headmask[:, :], compare_op=ALU.is_ge, fill=0.0,
                               base=0, pattern=[[-HD, HPC]], channel_multiplier=1).then_inc(const_base, 1)
            pool.wait_ge(const_base, 8)
            pool.affine_select(out=headmask[:, :], in_=headmask[:, :], compare_op=ALU.is_ge, fill=0.0,
                               base=HD - 1, pattern=[[HD, HPC]], channel_multiplier=-1).then_inc(const_made, 1)
            pool.affine_select(out=causal[:, :], in_=causal[:, :], compare_op=ALU.is_ge, fill=MASKED,
                               base=0, pattern=[[-1, P]], channel_multiplier=1).then_inc(const_made, 1)
            pool.affine_select(out=before[:, :], in_=before[:, :], compare_op=ALU.is_ge, fill=0.0,
                               base=-1, pattern=[[1, P]], channel_multiplier=-1).then_inc(const_made, 1)
            pool.affine_select(out=slot_no[:, :], in_=slot_no[:, :], compare_op=ALU.is_ge, fill=-1.0,
                               base=CAP - 1, pattern=[[-1, SLOTS]], channel_multiplier=0).then_inc(const_made, 1)
            for c in range(2 * DC):
                pool.wait_ge(rrow_ready, c + 1)
                pool.tensor_tensor(prob[:, c % DC], prob[:, c % DC],
                                   rrow[:, c].unsqueeze(2).to_broadcast([P, HPC, P]),
                                   ALU.mult).then_inc(prob_ready, 1)

        @block.scalar
        def _(act):
            def norm_std(n):
                act.wait_ge(eps_added, n + 1)
                act.activation(std[:, n:n + 1], meanvar[:, n, 1:2], ACT.Sqrt).then_inc(std_made, 1)

            def copy_xnT(n):
                act.wait_ge(xnT_psum, n + 1)
                act.copy(xnT[:, 2:4, :], ps_xT[1][:, 0:2 * P].rearrange("p (c t) -> p c t", c=2))\
                   .then_inc(xnT_b, 1)

            act.wait_ge(warm_set, 1)
            norm_std(0)
            act.activation(warm[:, 1:2], warm[:, 0:1], ACT.Exp)

            for a in range(2):
                copy_xnT(a)

                def copy_q(m):
                    c = DC * a + m
                    act.wait_ge(q_psum, c + 1)
                    act.copy(qT[:, m, :], ps_q[:, 0:P]).then_inc(q_ready, 1)

                def exp(m):
                    c = DC * a + m
                    act.wait_ge(nmax_ready, c + 1)
                    for k in range(HPC):
                        last = act.activation(prob[:, m, k, :], prob[:, m, k, :], ACT.Exp,
                                              bias=nmax[:, c, k:k + 1], accum_out=rowsum[:, c, k:k + 1])
                    last.then_inc(exp_done, 1)

                def copy_probT(m):
                    c = DC * a + m
                    act.wait_ge(probT_psum, c + 1)
                    if c >= 2:
                        act.wait_ge(o_psum, c - 1)
                    act.copy(probT[:, c % 2], ps_t[:, :].rearrange("p (h q) -> p h q", h=HPC))\
                       .then_inc(probT_ready, 1)

                copy_q(0)
                copy_q(1)
                copy_q(2)
                exp(0)
                copy_q(3)
                exp(1)
                copy_probT(0)
                exp(2)
                copy_probT(1)
                exp(3)
                act.activation(warm[:, 1:2], warm[:, 0:1], ACT.Sqrt)
                copy_probT(2)
                copy_probT(3)
                norm_std(a + 1)
                act.activation(warm[:, 1:2], warm[:, 0:1], ACT.Exp)

            copy_xnT(2)
            act.wait_ge(route, 1)
            act.activation(lexp[:, :], ps_r[:, 0:E], ACT.Exp, bias=lmax[:, :], accum_out=lsum[:, :])\
               .then_inc(lexp_ready, 1)
            act.activation(warm[:, 1:2], warm[:, 0:1], ACT.Silu)

            def silu_of(job):
                act.wait_ge(gate_psum, job + 1)
                act.activation(silu, ps_g[:, 0:F], ACT.Silu).then_inc(silu_ready, 1)

            def copy_hT(job):
                act.wait_ge(hT_psum, job + 1)
                act.copy(hsT[:, 0:3 * P], ps_h[:, 0:3 * P])
                act.copy(hsT[0:FT, 3 * P:4 * P], ps_h[0:FT, 3 * P:4 * P]).then_inc(hT_ready, 1)

            def copy_shared_hT(job):
                act.wait_ge(hT_psum, job + 1)
                act.copy(hsT[:, 0:2 * P], ps_h[:, 0:2 * P])
                act.copy(hsT[0:FT, 3 * P:4 * P], ps_h[0:FT, 3 * P:4 * P]).then_inc(hT_ready, 1)

            def copy_xe(p):
                act.wait_ge(xe_psum, p + 1)
                act.copy(xeT[:, 2:4, :], ps_xe[1][:, 0:2 * P].rearrange("p (c s) -> p c s", c=2))\
                   .then_inc(xe_b, 1)

            silu_of(0)
            act.wait_ge(h_ready, 1)
            silu_of(1)
            copy_shared_hT(0)
            copy_xe(0)
            act.wait_ge(down_done, 1)
            copy_shared_hT(1)
            act.wait_ge(h_ready, 2)
            silu_of(2)

            def pair_step(p):
                copy_xe(p + 1)
                copy_hT(p + 2)
                act.wait_ge(h_ready, p + 3)
                silu_of(p + 3)

            with act.Fori(0, 3) as i:
                for j in range(RING):
                    pair_step(i * RING + j)
            copy_hT(PAIRS + 1)

        @block.vector
        def _(dve):
            dve.memset(warm[:, 0:1], 1.0).then_inc(warm_set, 1)
            dve.memset(top[:, 6:7], -1.0)
            dve.memset(top[:, 7:8], -2.0)

            def layer_norm(n):
                dve.bn_stats(stats[:, n], x[:, :]).then_inc(stats_made, 1)
                dve.wait_ge(stats_made, n + 1)
                dve.bn_aggr(meanvar[:, n], stats[:, n]).then_inc(meanvar_made, 1)
                dve.wait_ge(meanvar_made, n + 1)
                dve.tensor_scalar(meanvar[:, n, 1:2], meanvar[:, n, 1:2], EPS, None, ALU.add)\
                   .then_inc(eps_added, 1)
                dve.wait_ge(std_made, n + 1)
                dve.reciprocal(rstd[:, n:n + 1], std[:, n:n + 1]).then_inc(rstd_made, 1)
                dve.wait_ge(rstd_made, n + 1)
                dve.tensor_scalar(xn[:, :], x[:, :], meanvar[:, n, 0:1], rstd[:, n:n + 1],
                                  ALU.subtract, ALU.mult).then_inc(xn_ready, 1)
                dve.wait_ge(xnT_psum, n + 1)
                dve.tensor_copy(xnT[:, 0:2, :], ps_xT[0][:, 0:2 * P].rearrange("p (c t) -> p c t", c=2))\
                   .then_inc(xnT_a, 1)

            dve.wait_ge(x_in, 16)
            layer_norm(0)
            for a in range(2):
                def spread_k(m):
                    c = DC * a + m
                    if a == 0:
                        dve.wait_ge(k_psum, 1)
                        dve.wait_ge(const_made, 5)
                        src = ps_k[:, m * P:(m + 1) * P]
                    else:
                        dve.wait_ge(k_psum, m + 2)
                        src = ps_k[:, 0:P]
                    if c >= 2:
                        dve.wait_ge(s_psum, c - 1)
                    dve.tensor_tensor(kx[:, c % 2], src.unsqueeze(1).to_broadcast([P, HPC, P]),
                                      headmask[:, :].unsqueeze(2).to_broadcast([P, HPC, P]),
                                      ALU.mult).then_inc(k_ready, 1)

                def mask(m):
                    c = DC * a + m
                    dve.wait_ge(s_psum, c + 1)
                    if c >= DC:
                        dve.wait_ge(probT_psum, c - DC + 1)
                    dve.scalar_tensor_tensor(prob[:, m], ps_s[c % 2][:, :].rearrange("p (h k) -> p h k", h=HPC),
                                             SCALE, causal[:, :].unsqueeze(1).to_broadcast([P, HPC, P]),
                                             ALU.mult, ALU.add).then_inc(s_masked, 1)
                    dve.wait_ge(s_masked, c + 1)
                    dve.tensor_reduce(nmax[:, c], prob[:, m], AX_X, ALU.max, negate=True)\
                       .then_inc(nmax_ready, 1)

                def invert(m):
                    c = DC * a + m
                    dve.wait_ge(exp_done, c + 1)
                    dve.reciprocal(rrow[:, c], rowsum[:, c]).then_inc(rrow_ready, 1)

                def copy_o(m):
                    c = DC * a + m
                    dve.wait_ge(o_psum, c + 1)
                    dve.tensor_copy(oT[:, m, :], ps_o[:, m * P:(m + 1) * P]).then_inc(o_ready, 1)

                def copy_v():
                    dve.wait_ge(v_psum, a + 1)
                    dve.tensor_copy(v, ps_v[:, :]).then_inc(v_ready, 1)

                if a == 0:
                    copy_v()
                spread_k(0)
                spread_k(1)
                mask(0)
                if a == 1:
                    copy_v()
                spread_k(2)
                mask(1)
                invert(0)
                spread_k(3)
                mask(2)
                invert(1)
                mask(3)
                copy_o(0)
                invert(2)
                copy_o(1)
                invert(3)
                copy_o(2)
                copy_o(3)
                dve.wait_ge(z_psum, a + 1)
                dve.tensor_tensor(x[:, :], ps_z[:, :], x[:, :], ALU.add).then_inc(x_ready, 1)
                dve.wait_ge(x_ready, a + 1)
                layer_norm(a + 1)

            step = [0]

            def then(ins):
                step[0] += 1
                ins.then_inc(route, 1)
                dve.wait_ge(route, step[0])

            dve.wait_ge(logits, 1)
            then(dve.tensor_reduce(lmax[:, :], ps_r[:, 0:E], AX_X, ALU.max, negate=True))
            dve.wait_ge(lexp_ready, 1)
            then(dve.reciprocal(rlsum[:, :], lsum[:, :]))
            then(dve.tensor_scalar(score[:, 0:E], lexp[:, :], rlsum[:, :], None, ALU.mult))
            then(dve.max(lexp[:, 0:8], score[:, 0:E]))
            then(dve.tensor_copy(top[:, 0:TOP_K], lexp[:, 0:TOP_K]))
            then(dve.match_replace(rest[:, :], top[:, :], score[:, :], -3.0))
            dve.tensor_scalar(chosen[:, :], rest[:, 0:E], 0.0, None, ALU.is_lt).then_inc(chosen_ready, 1)
            then(dve.tensor_reduce(wsum[:, :], top[:, 0:TOP_K], AX_X, ALU.add))
            then(dve.tensor_scalar(wsum[:, :], wsum[:, :], 1e-20, None, ALU.add))
            then(dve.reciprocal(rwsum[:, :], wsum[:, :]))
            then(dve.tensor_scalar(weight[:, :], score[:, 0:E], rwsum[:, :], None, ALU.mult))
            dve.wait_ge(chosen_ready, 1)
            dve.wait_ge(count_psum, 1)
            then(dve.scalar_tensor_tensor(place[:, :], ps_r[:, 0:E], 1.0, chosen[:, :], ALU.add, ALU.mult))

            def column(t, e):
                return t[:, bass.ds(e, 1)]

            def make_gather(p):
                for e in range(2):
                    last = dve.tensor_scalar(gather[:, e * SLOTS:(e + 1) * SLOTS], slot_no[:, :],
                                             column(place, p * 2 + e), None, ALU.is_equal)
                last.then_inc(gather_ready, 1)

            def make_scatter(p):
                for e in range(2):
                    last = dve.tensor_scalar(scatter[:, e * SLOTS:(e + 1) * SLOTS], slot_no[:, :],
                                             column(place, p * 2 + e), column(weight, p * 2 + e),
                                             ALU.is_equal, ALU.mult)
                last.then_inc(scatter_ready, 1)

            def gate_up(job):
                dve.wait_ge(silu_ready, job + 1)
                dve.wait_ge(up_psum, job + 1)
                dve.tensor_tensor(h, ps_u[:, 0:F], silu, ALU.mult).then_inc(h_ready, 1)

            def copy_xe(p):
                dve.wait_ge(xe_psum, p + 1)
                dve.tensor_copy(xeT[:, 0:2, :], ps_xe[0][:, 0:2 * P].rearrange("p (c s) -> p c s", c=2))\
                   .then_inc(xe_a, 1)

            def copy_ye(p):
                dve.wait_ge(down_done, p + 3)
                dve.tensor_copy(ye, ps_ye[:, :]).then_inc(ye_ready, 1)

            make_gather(0)
            gate_up(0)
            dve.wait_ge(hT_psum, 1)
            gate_up(1)
            copy_xe(0)

            def pair_step(p):
                make_gather(p + 1)
                dve.wait_ge(hT_psum, p + 2)
                make_scatter(p)
                gate_up(p + 2)
                copy_xe(p + 1)
                copy_ye(p)

            with dve.Fori(0, 3) as i:
                for j in range(RING):
                    pair_step(i * RING + j)
            dve.wait_ge(hT_psum, PAIRS + 1)
            make_scatter(PAIRS - 1)
            gate_up(PAIRS + 1)
            copy_ye(PAIRS - 1)
            dve.wait_ge(y_psum, 1)
            dve.tensor_tensor(final, ps_y[:, :], x[:, :], ALU.add).then_inc(final_ready, 1)

        @block.tensor
        def _(pe):
            def transpose_xn(n):
                pe.wait_ge(xn_ready, n + 1)
                for c in range(DC):
                    last = pe.transpose(ps_xT[c // 2][:, (c % 2) * P:(c % 2 + 1) * P],
                                        xn[:, c * P:(c + 1) * P], ident[:, :])
                last.then_inc(xnT_psum, 1)

            pe.wait_ge(kv_in, 32)
            for m in range(DC):
                last = pe.matmul(ps_k[:, m * P:(m + 1) * P], kv_w[:, m * P:(m + 1) * P], ctxT[:, :],
                                 start=True, stop=True)
            last.then_inc(k_psum, 1)
            pe.matmul(ps_v[:, :], ctxT[:, :], kv_w[:, D:2 * D], start=True, stop=True).then_inc(v_psum, 1)
            pe.wait_ge(const_made, 5)
            transpose_xn(0)

            for a in range(2):
                pe.wait_ge(xnT_a, a + 1)
                pe.wait_ge(xnT_b, a + 1)
                pe.wait_ge(q_in[a], 16)

                def project(m):
                    c = DC * a + m
                    if m >= 1:
                        pe.wait_ge(q_ready, c)
                    for k in range(DC):
                        last = pe.matmul(ps_q[:, 0:P], q_w[a][:, k, m * P:(m + 1) * P], xnT[:, k, :],
                                         start=(k == 0), stop=(k == DC - 1))
                    last.then_inc(q_psum, 1)
                    if a == 1:
                        if m == 0:
                            pe.wait_ge(aw_in[1], 16)
                        pe.wait_ge(k_ready, c)
                        for k in range(DC):
                            last = pe.matmul(ps_k[:, 0:P], a_w[1][:, k, m * P:(m + 1) * P], xnT[:, k, :],
                                             start=(k == 0), stop=(k == DC - 1))
                        last.then_inc(k_psum, 1)

                def values():
                    pe.wait_ge(aw_in[2], 16)
                    for k in range(DC):
                        last = pe.matmul(ps_v[:, :], xnT[:, k, :], a_w[2][:, k, :],
                                         start=(k == 0), stop=(k == DC - 1))
                    last.then_inc(v_psum, 1)

                def scores(m):
                    c = DC * a + m
                    pe.wait_ge(q_ready, c + 1)
                    pe.wait_ge(k_ready, c + 1)
                    if c >= 2:
                        pe.wait_ge(s_masked, c - 1)
                    pe.matmul(ps_s[c % 2][:, :], qT[:, m, :], kx[:, c % 2], start=True, stop=True)\
                      .then_inc(s_psum, 1)

                def transpose_prob(m):
                    c = DC * a + m
                    pe.wait_ge(prob_ready, c + 1)
                    if c >= 1:
                        pe.wait_ge(probT_ready, c)
                    for k in range(HPC):
                        last = pe.transpose(ps_t[:, k * P:(k + 1) * P], prob[:, m, k, :], ident[:, :])
                    last.then_inc(probT_psum, 1)

                def weighted_values(m):
                    c = DC * a + m
                    pe.wait_ge(probT_ready, c + 1)
                    pe.wait_ge(v_ready, a + 1)
                    if c >= 1:
                        pe.wait_ge(o_ready, c)
                    for k in range(HPC):
                        n = (m * HPC + k) * HD
                        last = pe.matmul(ps_o[k * HD:(k + 1) * HD, m * P:(m + 1) * P], v[:, n:n + HD],
                                         probT[:, c % 2, k, :], start=True, stop=True)
                    last.then_inc(o_psum, 1)

                def output(m):
                    c = DC * a + m
                    pe.wait_ge(o_ready, c + 1)
                    if m == 0:
                        pe.wait_ge(o_in[a], 16)
                    last = pe.matmul(ps_z[:, :], oT[:, m, :], o_w[a][:, m, :],
                                     start=(m == 0), stop=(m == DC - 1))
                    if m == DC - 1:
                        last.then_inc(z_psum, 1)

                project(0)
                project(1)
                scores(0)
                project(2)
                scores(1)
                if a == 1:
                    values()
                project(3)
                scores(2)
                transpose_prob(0)
                scores(3)
                weighted_values(0)
                transpose_prob(1)
                output(0)
                weighted_values(1)
                transpose_prob(2)
                output(1)
                weighted_values(2)
                transpose_prob(3)
                output(2)
                weighted_values(3)
                output(3)
                transpose_xn(a + 1)

            pe.wait_ge(xnT_a, LN)
            pe.wait_ge(xnT_b, LN)
            pe.wait_ge(wg_in, 16)
            for k in range(DC):
                last = pe.matmul(ps_r[:, 0:E], xnT[:, k, :], wg[:, k, :], start=(k == 0), stop=(k == DC - 1))
            last.then_inc(logits, 1)

            def shared_in(half, w, out, landed, done):
                if half == 0:
                    pe.wait_ge(landed, 16)
                for k in range(DC):
                    last = pe.matmul(out[:, 0:F], xnT[:, k, :], w[:, k, half, :],
                                     start=(k == 0), stop=(k == DC - 1))
                last.then_inc(done, 1)

            def transpose_h():
                for c in range(2):
                    pe.transpose(ps_h[:, c * P:(c + 1) * P], h[:, c * P:(c + 1) * P], ident[:, :])
                return pe.transpose(ps_h[0:FT, 3 * P:4 * P], h[:, 2 * P:F], ident[:, :])

            def shared_down(half):
                pe.wait_ge(hT_ready, half + 1)
                if half == 0:
                    pe.wait_ge(down_in[0], 16)
                    pe.wait_ge(tail_in[0], 16)
                for c in range(2):
                    pe.matmul(ps_y[:, :], hsT[:, c * P:(c + 1) * P], down_w(0)[:, c, half, :],
                              start=(half == 0 and c == 0), stop=False)
                pe.matmul(ps_y[:, :], hsT[0:FT, 3 * P:4 * P], tail_w(0)[:, half, :],
                          start=False, stop=False).then_inc(down_done, 1)

            def gather_tokens(p):
                pe.wait_ge(gather_ready, p + 1)
                for c in range(DC):
                    last = pe.matmul(ps_xe[c // 2][:, (c % 2) * P:(c % 2 + 1) * P], xn[:, c * P:(c + 1) * P],
                                     gather, start=True, stop=True)
                last.then_inc(xe_psum, 1)

            def pair_in(k, w, out):
                for e in range(2):
                    rows = slice(e * SLOTS, (e + 1) * SLOTS)
                    last = pe.matmul(out[rows, 0:F], xeT[:, k, rows], w[:, k, e, :],
                                     start=(k == 0), stop=(k == DC - 1))
                return last

            def pair_gate_begin(p, s, use):
                pe.wait_ge(xe_a, p + 1)
                pe.wait_ge(xe_b, p + 1)
                pe.wait_ge(gate_in[s], use * 16)
                pe.wait_ge(silu_ready, p + 2)
                pair_in(0, gate_w(s), ps_g)
                pair_in(1, gate_w(s), ps_g)

            def pair_gate_end(s):
                pair_in(2, gate_w(s), ps_g)
                pair_in(3, gate_w(s), ps_g).then_inc(gate_psum, 1)

            def pair_up(p, s, use):
                pe.wait_ge(up_in[s], use * 16)
                pe.wait_ge(h_ready, p + 2)
                for k in range(DC):
                    last = pair_in(k, up_w(s), ps_u)
                last.then_inc(up_psum, 1)

            def pair_transposes(p):
                pe.wait_ge(scatter_ready, p + 1)
                pe.wait_ge(hT_ready, p + 2)
                pe.transpose(ps_h[:, 2 * P:3 * P], scatter, ident[:, :])
                pe.wait_ge(h_ready, p + 3)
                transpose_h().then_inc(hT_psum, 1)

            def pair_down(p, s, use):
                pe.wait_ge(hT_ready, p + 3)
                pe.wait_ge(down_in[s], use * 16)
                for c in range(2):
                    for e in range(2):
                        rows = slice(e * SLOTS, (e + 1) * SLOTS)
                        at = c * P + e * SLOTS
                        pe.matmul(ps_ye[rows, :], hsT[:, at:at + SLOTS], down_w(s)[:, c, e, :],
                                  start=(c == 0), stop=False)
                pe.wait_ge(tail_in[s], use * 16)
                for e in range(2):
                    rows = slice(e * SLOTS, (e + 1) * SLOTS)
                    at = 3 * P + e * SLOTS
                    last = pe.matmul(ps_ye[rows, :], hsT[0:FT, at:at + SLOTS], tail_w(s)[:, e, :],
                                     start=False, stop=True)
                last.then_inc(down_done, 1)

            def add_pair(p, last_pair):
                pe.wait_ge(ye_ready, p + 1)
                return pe.matmul(ps_y[:, :], hsT[:, 2 * P:3 * P], ye, start=False, stop=last_pair)

            shared_in(0, gate_w(0), ps_g, gate_in[0], gate_psum)
            shared_in(0, up_w(0), ps_u, up_in[0], up_psum)
            pe.wait_ge(chosen_ready, 1)
            pe.wait_ge(lexp_ready, 1)
            pe.matmul(ps_r[:, 0:E], before[:, :], chosen[:, :], start=True, stop=True).then_inc(count_psum, 1)
            pe.wait_ge(silu_ready, 1)
            shared_in(1, gate_w(0), ps_g, gate_in[0], gate_psum)
            pe.wait_ge(h_ready, 1)
            transpose_h().then_inc(hT_psum, 1)
            shared_in(1, up_w(0), ps_u, up_in[0], up_psum)
            shared_down(0)
            gather_tokens(0)
            pe.wait_ge(h_ready, 2)
            transpose_h().then_inc(hT_psum, 1)
            pair_gate_begin(0, 1, 1)
            shared_down(1)
            pair_gate_end(1)

            def pair_step(p, i, j):
                s, t = (j + 1) % RING, (j + 2) % RING
                pair_up(p, s, i + 1 + (j + 1) // RING)
                gather_tokens(p + 1)
                pair_transposes(p)
                pair_gate_begin(p + 1, t, i + 1 + (j + 2) // RING)
                pair_down(p, s, i + 1 + (j + 1) // RING)
                pair_gate_end(t)
                add_pair(p, False)

            with pe.Fori(0, 3) as i:
                for j in range(RING):
                    pair_step(i * RING + j, i, j)
            last = PAIRS - 1
            s, use = PAIRS % RING, PAIRS // RING + 1
            pair_up(last, s, use)
            pair_transposes(last)
            pair_down(last, s, use)
            add_pair(last, True).then_inc(y_psum, 1)


def kernel(x, ctx_512, L0_xattn_Wq, L0_xattn_Wkv_expand, L0_xattn_Wout, L0_attn_Wq, L0_attn_Wk, L0_attn_Wv,
           L0_attn_Wo, L0_ffn_wg_router, L0_ffn_w_gate, L0_ffn_w_up, L0_ffn_w_down, L0_ffn_ws_gate,
           L0_ffn_ws_up, L0_ffn_ws_down):
    import numpy as np
    import concourse.bacc as bacc
    from concourse.bass_utils import run_bass_kernel_spmd

    def chunks(w):
        w = np.asarray(w)
        return w.reshape(-1, P, w.shape[-1]).transpose(1, 0, 2).reshape(P, -1)

    def expert_slots(gate, up, down):
        n = gate.shape[0]

        def w_in(w):
            return w.reshape(n, 2, DC, P, F).transpose(0, 3, 2, 1, 4).reshape(n, P, GATE)

        main = down[:, :, :2 * P].reshape(n, 2, 2, P, D).transpose(0, 3, 2, 1, 4).reshape(n, P, 4 * D)
        tail = down[:, :, 2 * P:].transpose(0, 2, 1, 3).reshape(n, FT, 2 * D)
        return np.concatenate([w_in(gate), w_in(up), main], axis=2), tail

    def halves(w):
        return np.asarray(w).reshape(1, D, 2, F).transpose(0, 2, 1, 3)

    pair, pair_tail = expert_slots(
        np.asarray(L0_ffn_w_gate).reshape(PAIRS, 2, D, F), np.asarray(L0_ffn_w_up).reshape(PAIRS, 2, D, F),
        np.asarray(L0_ffn_w_down).reshape(PAIRS, 2, F, D))
    shared, shared_tail = expert_slots(
        halves(L0_ffn_ws_gate), halves(L0_ffn_ws_up), np.asarray(L0_ffn_ws_down).reshape(1, 2, F, D))
    arrays = {
        "x_d": np.asarray(x)[0],
        "ctxT_d": np.asarray(ctx_512)[0, :P].T,
        "xw_d": np.concatenate([chunks(np.asarray(L0_xattn_Wq).T), np.asarray(L0_xattn_Wkv_expand).T,
                                chunks(np.asarray(L0_xattn_Wout).T)], axis=1),
        "aw_d": np.concatenate([chunks(np.asarray(w).T) for w in (L0_attn_Wq, L0_attn_Wk, L0_attn_Wv,
                                                                  L0_attn_Wo)], axis=1),
        "wg_d": chunks(np.asarray(L0_ffn_wg_router).T),
        "sh_d": shared[0], "sh_tail_d": shared_tail[0],
        "pair_d": pair, "pair_tail_d": pair_tail,
    }
    arrays = {name: np.ascontiguousarray(a) for name, a in arrays.items()}
    nc = bacc.Bacc("TRN2", target_bir_lowering=False, num_devices=1)
    args = [nc.dram_tensor(name, a.shape, mybir.dt.from_np(a.dtype), kind="ExternalInput").ap()
            for name, a in arrays.items()]
    args.append(nc.dram_tensor("out_d", [P, D], F32, kind="ExternalOutput").ap())
    perceiver_layer(nc, *args)
    r = run_bass_kernel_spmd(nc, [arrays], core_ids=[0])
    return np.asarray(r.results[0]["out_d"]).reshape(1, P, D)
```

```python
from contextlib import ExitStack

import concourse.bass as bass
from concourse import mybir

F32 = mybir.dt.float32
F32R = mybir.dt.float32r
BF16 = mybir.dt.bfloat16
ALU = mybir.AluOpType
ACT = mybir.ActivationFunctionType
AX_X = mybir.AxisListType.X

P = 128
D = 512
DC = D // P
NH = 16
HD = D // NH
HPC = P // HD
E = 32
TOP_K = 6
CAP = 2 * (P * TOP_K // E)
SLOTS = 64
F = 352
FT = F - 2 * P
PAIRS = E // 2
RING = 5
GATE = DC * 2 * F
UP0 = GATE
DOWN0 = 2 * GATE
TAIL0 = DOWN0 + 2 * 2 * D
SLOT = TAIL0 + 2 * D
ROUTER = DC * E
XW = DC * D + 2 * D + DC * D
AW = 4 * DC * D
SCALE = 1.0 / float(HD) ** 0.5
EPS = 1e-5
MASKED = -3.4028234663852886e38
LN = 3


def perceiver_layer(nc, x_d, ctxT_d, xw_d, aw_d, sh_d, sh_tail_d, pair_d, pair_tail_d, out_d):
    ctx = ExitStack()
    with ctx:
        def sb(name, shape, dtype=F32):
            return ctx.enter_context(nc.sbuf_tensor(name, shape, dtype))

        def sem(name):
            return ctx.enter_context(nc.semaphore(name))

        ring = sb("ring", [P, ROUTER + RING * SLOT])
        x = sb("x", [P, D])
        xn = sb("xn", [P, D])
        xnT = sb("xnT", [P, DC, P])
        ctxT = sb("ctxT", [P, P])
        ident = sb("ident", [P, P])
        before = sb("before", [P, P])
        causal = sb("causal", [P, P])
        headmask = sb("headmask", [P, HPC])
        slot_no = sb("slot_no", [P, SLOTS])
        stats = sb("stats", [P, LN, 2, 6])
        meanvar = sb("meanvar", [P, LN, 2])
        std = sb("std", [P, LN])
        rstd = sb("rstd", [P, LN])
        warm = sb("warm", [P, 2])
        ones = sb("ones", [P, P], BF16)
        warmed = sb("warmed", [P, 7])
        nmax = sb("nmax", [P, 2 * DC, HPC])
        rowsum = sb("rowsum", [P, 2 * DC, HPC])
        rrow = sb("rrow", [P, 2 * DC, HPC])
        lmax = sb("lmax", [P, 1])
        lsum = sb("lsum", [P, 1])
        rlsum = sb("rlsum", [P, 1])
        lexp = sb("lexp", [P, E])
        score = sb("score", [P, E + 2])
        top = sb("top", [P, 8])
        rest = sb("rest", [P, E + 2])
        chosen = sb("chosen", [P, E])
        wsum = sb("wsum", [P, 1])
        rwsum = sb("rwsum", [P, 1])
        weight = sb("weight", [P, E])
        place = sb("place", [P, E])
        arena = sb("arena", [P, 4608])

        def part(at, n):
            return arena[:, at:at + n]

        qT = part(0, 512).rearrange("p (c t) -> p c t", c=DC)
        kx = part(512, 1024).rearrange("p (b h k) -> p b h k", b=2, h=HPC)
        prob = part(1536, 2048).rearrange("p (b h k) -> p b h k", b=DC, h=HPC)
        probT = part(3584, 1024).rearrange("p (b h q) -> p b h q", b=2, h=HPC)
        oT = qT

        xeT = part(0, 512).rearrange("p (c s) -> p c s", c=DC)
        silu = part(512, 352)
        h = part(864, 352)
        hT = part(1216, 3 * P)
        scatter = part(2368, 128)
        final = part(2496, 512)
        x_rest = part(3008, 512)
        x_parts = sb("x_parts", [P, 3, D], BF16)
        ye_hi = sb("ye_hi", [P, D], F32R)
        ye_lo = sb("ye_lo", [P, D], F32R)
        gather = sb("gather", [P, P], BF16)
        slots = sb("slots", [P, P], F32R)
        slot_w = sb("slot_w", [P, 1])

        bank = [ctx.enter_context(nc.psum_tensor(f"bank{i}", [P, 512], F32)) for i in range(8)]
        ps_o, ps_t, ps_q, ps_k, ps_v = bank[1], bank[4], bank[5], bank[6], bank[7]
        ps_s = [bank[2], bank[3]]
        ps_z = [bank[0], bank[2]]
        ps_xT = [bank[4], bank[3]]
        ps_xe = [bank[2], bank[3]]
        ps_g, ps_u, ps_h, ps_ye, ps_y, ps_r = bank[4], bank[5], bank[6], bank[7], bank[0], bank[1]
        ps_sc = ps_r

        x_in = sem("x_in")
        k_in = sem("k_in")
        v_in = sem("v_in")
        xq_in = sem("xq_in")
        xo_in = sem("xo_in")
        aw_in = [sem(f"aw{n}_in") for n in range(4)]
        gate_in = [sem(f"gate_in{s}") for s in range(RING)]
        up_in = [sem(f"up_in{s}") for s in range(RING)]
        down_in = [sem(f"down_in{s}") for s in range(RING)]
        tail_in = [sem(f"tail_in{s}") for s in range(RING)]
        out_done = sem("out_done")
        const_base = sem("const_base")
        const_made = sem("const_made")
        warm_set = sem("warm_set")
        ones_set = sem("ones_set")
        x_ready = sem("x_ready")
        stats_made = sem("stats_made")
        meanvar_made = sem("meanvar_made")
        std_made = sem("std_made")
        rstd_made = sem("rstd_made")
        xn_ready = sem("xn_ready")
        xn_a = sem("xn_a")
        xnT_psum_a = sem("xnT_psum_a")
        xnT_psum_b = sem("xnT_psum_b")
        xnT_a = sem("xnT_a")
        xnT_b = sem("xnT_b")
        q_psum = sem("q_psum")
        q_ready = sem("q_ready")
        k_psum = sem("k_psum")
        k_ready = sem("k_ready")
        v_psum = sem("v_psum")
        v_ready = sem("v_ready")
        s_psum = sem("s_psum")
        s_masked = sem("s_masked")
        nmax_ready = sem("nmax_ready")
        exp_done = sem("exp_done")
        rrow_ready = sem("rrow_ready")
        prob_ready = sem("prob_ready")
        last_prob_ready = sem("last_prob_ready")
        probT_psum = sem("probT_psum")
        probT_ready = sem("probT_ready")
        o_psum = sem("o_psum")
        o_ready = sem("o_ready")
        z_psum_a = sem("z_psum_a")
        z_psum = sem("z_psum")
        route = sem("route")
        lexp_ready = sem("lexp_ready")
        chosen_ready = sem("chosen_ready")
        count_psum = sem("count_psum")
        gate_psum = sem("gate_psum")
        up_psum = sem("up_psum")
        silu_ready = sem("silu_ready")
        h_ready = sem("h_ready")
        hT_psum = sem("hT_psum")
        hT_ready = sem("hT_ready")
        down_done = sem("down_done")
        gather_ready = sem("gather_ready")
        scatter_ready = sem("scatter_ready")
        xe_psum_a = sem("xe_psum_a")
        xe_psum_b = sem("xe_psum_b")
        xe_a = sem("xe_a")
        xe_b = sem("xe_b")
        ye_hi_ready = sem("ye_hi_ready")
        ye_ready = sem("ye_ready")
        scatter_psum = sem("scatter_psum")
        slot_w_ready = sem("slot_w_ready")
        slots_ready = sem("slots_ready")
        x_part = [sem(f"x_part{n}") for n in range(3)]
        x_rest_ready = sem("x_rest_ready")
        y_psum = sem("y_psum")
        final_ready = sem("final_ready")

        def slot(s, at, n):
            return ring[:, ROUTER + s * SLOT + at:ROUTER + s * SLOT + at + n]

        def gate_w(s):
            return slot(s, 0, GATE).rearrange("p (c e f) -> p c e f", c=DC, e=2)

        def up_w(s):
            return slot(s, UP0, GATE).rearrange("p (c e f) -> p c e f", c=DC, e=2)

        def down_w(s):
            return slot(s, DOWN0, 4 * D).rearrange("p (c e n) -> p c e n", c=2, e=2)

        def tail_w(s):
            return slot(s, TAIL0, 2 * D)[0:FT].rearrange("p (e n) -> p e n", e=2)

        shared_gate_w = [ring[:, 0:ROUTER + DC * F].rearrange("p (c f) -> p c f", c=DC),
                         slot(0, DC * F, DC * F).rearrange("p (c f) -> p c f", c=DC)]

        v = slot(4, AW, D)
        xq_w = slot(3, 0, DC * D).rearrange("p (c n) -> p c n", c=DC)
        kv_w = slot(3, DC * D, 2 * D)
        xo_w = slot(3, DC * D + 2 * D, DC * D).rearrange("p (c n) -> p c n", c=DC)
        a_w = [slot(4, n * DC * D, DC * D).rearrange("p (c n) -> p c n", c=DC) for n in range(4)]
        q_w, o_w = [xq_w, a_w[0]], [xo_w, a_w[3]]
        q_in, o_in = [xq_in, aw_in[0]], [xo_in, aw_in[3]]

        block = ctx.enter_context(nc.Block())

        @block.sync
        def _(sp):
            sp.dma_start(x[:, :], x_d).then_inc(x_in, 16)
            sp.dma_start(ctxT[:, :], ctxT_d).then_inc(k_in, 16)
            sp.dma_start(slot(3, DC * D, D), xw_d[:, DC * D:DC * D + D]).then_inc(k_in, 16)
            sp.dma_start(slot(3, 0, DC * D), xw_d[:, 0:DC * D]).then_inc(xq_in, 16)
            sp.dma_start(slot(3, DC * D + D, D), xw_d[:, DC * D + D:DC * D + 2 * D]).then_inc(v_in, 16)
            sp.dma_start(slot(3, DC * D + 2 * D, DC * D), xw_d[:, DC * D + 2 * D:XW]).then_inc(xo_in, 16)
            for n in range(4):
                sp.dma_start(slot(4, n * DC * D, DC * D),
                             aw_d[:, n * DC * D:(n + 1) * DC * D]).then_inc(aw_in[n], 16)

            def load_gate(s, src):
                sp.dma_start(slot(s, 0, GATE), src[:, 0:GATE]).then_inc(gate_in[s], 16)

            def load_up(s, src):
                sp.dma_start(slot(s, UP0, GATE), src[:, UP0:UP0 + GATE]).then_inc(up_in[s], 16)

            def load_down(s, src, tail):
                sp.dma_start(slot(s, DOWN0, 4 * D), src[:, DOWN0:TAIL0]).then_inc(down_in[s], 16)
                sp.dma_start(slot(s, TAIL0, 2 * D)[0:FT], tail).then_inc(tail_in[s], 16)

            sp.dma_start(ring[:, 0:ROUTER + GATE], sh_d[:, 0:ROUTER + GATE]).then_inc(gate_in[0], 16)
            load_up(0, sh_d[:, ROUTER:])
            load_down(0, sh_d[:, ROUTER:], sh_tail_d)
            for p in range(RING - 1):
                s = p + 1
                if s == 3:
                    sp.wait_ge(z_psum, 1)
                if s == 4:
                    sp.wait_ge(z_psum, 2)
                load_gate(s, pair_d[p])
                load_up(s, pair_d[p])
                load_down(s, pair_d[p], pair_tail_d[p])

            def load_pair(p, s):
                src = pair_d[bass.ds(p, 1)].rearrange("a p n -> (a p) n")
                tail = pair_tail_d[bass.ds(p, 1)].rearrange("a p n -> (a p) n")
                sp.wait_ge(gate_psum, p - 2)
                load_gate(s, src)
                sp.wait_ge(up_psum, p - 2)
                load_up(s, src)
                sp.wait_ge(down_done, p - 2)
                load_down(s, src, tail)

            with sp.Fori(0, 2) as i:
                for j in range(RING):
                    load_pair(i * RING + (RING - 1 + j), j)
            for p in range(3 * RING - 1, PAIRS):
                load_pair(p, (p + 1) % RING)

            sp.wait_ge(final_ready, 1)
            sp.dma_start(out_d, final).then_inc(out_done, 16)
            sp.wait_ge(out_done, 16)

        @block.gpsimd
        def _(pool):
            pool.memset(ident[:, :], 0.0).then_inc(const_base, 1)
            pool.memset(before[:, :], 1.0).then_inc(const_base, 1)
            pool.memset(causal[:, :], 0.0).then_inc(const_base, 1)
            pool.memset(headmask[:, :], 1.0).then_inc(const_base, 1)
            pool.iota(slot_no[:, :], pattern=[[1, SLOTS]], base=1, channel_multiplier=0,
                      allow_small_or_imprecise_dtypes=True).then_inc(const_base, 1)
            pool.memset(score[:, E:E + 1], -1.0).then_inc(const_base, 1)
            pool.memset(score[:, E + 1:E + 2], -2.0).then_inc(const_base, 1)
            pool.wait_ge(const_base, 7)
            pool.affine_select(out=ident[:, :], in_=ident[:, :], compare_op=ALU.not_equal, fill=1.0,
                               base=0, pattern=[[-1, P]], channel_multiplier=1).then_inc(const_made, 1)
            pool.affine_select(out=headmask[:, :], in_=headmask[:, :], compare_op=ALU.is_ge, fill=0.0,
                               base=0, pattern=[[-HD, HPC]], channel_multiplier=1).then_inc(const_base, 1)
            pool.wait_ge(const_base, 8)
            pool.affine_select(out=headmask[:, :], in_=headmask[:, :], compare_op=ALU.is_ge, fill=0.0,
                               base=HD - 1, pattern=[[HD, HPC]], channel_multiplier=-1).then_inc(const_made, 1)
            pool.affine_select(out=causal[:, :], in_=causal[:, :], compare_op=ALU.is_ge, fill=MASKED,
                               base=0, pattern=[[-1, P]], channel_multiplier=1).then_inc(const_made, 1)
            pool.affine_select(out=before[:, :], in_=before[:, :], compare_op=ALU.is_ge, fill=0.0,
                               base=-1, pattern=[[1, P]], channel_multiplier=-1).then_inc(const_made, 1)
            pool.affine_select(out=slot_no[:, :], in_=slot_no[:, :], compare_op=ALU.is_ge, fill=-1.0,
                               base=CAP - 1, pattern=[[-1, SLOTS]], channel_multiplier=0).then_inc(const_made, 1)
            for c in (0, 1, 2, 4, 5, 6):
                pool.wait_ge(rrow_ready, c + 1)
                pool.tensor_tensor(prob[:, c % DC], prob[:, c % DC],
                                   rrow[:, c].unsqueeze(2).to_broadcast([P, HPC, P]),
                                   ALU.mult).then_inc(prob_ready, 1)

        @block.scalar
        def _(act):
            def norm_std(n):
                act.wait_ge(meanvar_made, n + 1)
                act.activation(std[:, n:n + 1], meanvar[:, n, 1:2], ACT.Sqrt, bias=warm[:, 1:2])\
                   .then_inc(std_made, 1)

            def copy_xnT(n):
                act.wait_ge(xnT_psum_b, n + 1)
                act.copy(xnT[:, 2:4, :], ps_xT[1][:, 0:2 * P].rearrange("p (c t) -> p c t", c=2))\
                   .then_inc(xnT_b, 1)

            act.wait_ge(warm_set, 2)
            act.activation(warmed[:, 0:1], warm[:, 0:1], ACT.Sqrt)
            norm_std(0)
            act.activation(warmed[:, 1:2], warm[:, 0:1], ACT.Exp)

            for a in range(2):
                copy_xnT(a)

                def copy_q(m):
                    c = DC * a + m
                    act.wait_ge(q_psum, c + 1)
                    act.copy(qT[:, m, :], ps_q[:, 0:P]).then_inc(q_ready, 1)

                def exp(m):
                    c = DC * a + m
                    act.wait_ge(nmax_ready, c + 1)
                    for k in range(HPC):
                        last = act.activation(prob[:, m, k, :], prob[:, m, k, :], ACT.Exp,
                                              bias=nmax[:, c, k:k + 1], accum_out=rowsum[:, c, k:k + 1])
                    last.then_inc(exp_done, 1)

                def copy_probT(m):
                    c = DC * a + m
                    act.wait_ge(probT_psum, c + 1)
                    if c >= 2:
                        act.wait_ge(o_psum, c - 1)
                    act.copy(probT[:, c % 2], ps_t[:, :].rearrange("p (h q) -> p h q", h=HPC))\
                       .then_inc(probT_ready, 1)

                copy_q(0)
                copy_q(1)
                copy_q(2)
                exp(0)
                copy_q(3)
                exp(1)
                copy_probT(0)
                exp(2)
                if a == 0:
                    copy_probT(1)
                    exp(3)
                else:
                    exp(3)
                    copy_probT(1)
                copy_probT(2)
                copy_probT(3)
                act.activation(warmed[:, 2 * a + 2:2 * a + 3], warm[:, 0:1], ACT.Sqrt)
                norm_std(a + 1)
                act.activation(warmed[:, 2 * a + 3:2 * a + 4], warm[:, 0:1], ACT.Exp)

            copy_xnT(2)
            act.copy(x_parts[:, 0, :], xn[:, :]).then_inc(x_part[0], 1)
            act.wait_ge(x_rest_ready, 1)
            act.copy(x_parts[:, 1, :], x_rest).then_inc(x_part[1], 1)
            act.wait_ge(route, 1)
            act.activation(lexp[:, :], ps_g[:, 0:E], ACT.Exp, bias=lmax[:, :], accum_out=lsum[:, :])\
               .then_inc(lexp_ready, 1)

            def silu_of(job, at=0):
                act.wait_ge(gate_psum, job + 1)
                act.activation(silu, ps_g[:, at:at + F], ACT.Silu).then_inc(silu_ready, 1)

            def copy_hT(job):
                act.wait_ge(hT_psum, job + 1)
                act.copy(hT[:, 0:2 * P], ps_h[:, 0:2 * P])
                act.copy(hT[0:FT, 2 * P:3 * P], ps_h[0:FT, 2 * P:3 * P]).then_inc(hT_ready, 1)

            def copy_ye_hi(p):
                act.wait_ge(down_done, p + 3)
                act.copy(ye_hi[:, :], ps_ye[:, :]).then_inc(ye_hi_ready, 1)

            def copy_xe(p):
                act.wait_ge(xe_psum_b, p + 1)
                act.copy(xeT[:, 2:4, :], ps_xe[1][:, 0:2 * P].rearrange("p (c s) -> p c s", c=2))\
                   .then_inc(xe_b, 1)

            silu_of(0, E)
            act.wait_ge(h_ready, 1)
            silu_of(1)
            copy_hT(0)
            copy_xe(0)
            act.wait_ge(down_done, 1)
            copy_hT(1)
            act.wait_ge(h_ready, 2)
            silu_of(2)

            def pair_step(p):
                copy_xe(p + 1)
                copy_hT(p + 2)
                copy_ye_hi(p)
                act.wait_ge(h_ready, p + 3)
                silu_of(p + 3)

            with act.Fori(0, 3) as i:
                for j in range(RING):
                    pair_step(i * RING + j)
            copy_hT(PAIRS + 1)
            copy_ye_hi(PAIRS - 1)

        @block.vector
        def _(dve):
            dve.memset(ones[:, :], 1.0).then_inc(ones_set, 1)
            dve.memset(warm[:, 0:1], 1.0).then_inc(warm_set, 1)
            dve.memset(warm[:, 1:2], EPS).then_inc(warm_set, 1)
            dve.memset(top[:, 6:7], -1.0)
            dve.memset(top[:, 7:8], -2.0)

            half = [slice(0, D // 2), slice(D // 2, D)]

            def take_stats(n, k):
                dve.bn_stats(stats[:, n, k], x[:, half[k]]).then_inc(stats_made, 1)

            def layer_norm(n):
                dve.wait_ge(stats_made, 2 * n + 2)
                dve.bn_aggr(meanvar[:, n], stats[:, n]).then_inc(meanvar_made, 1)
                dve.wait_ge(meanvar_made, n + 1)
                dve.wait_ge(std_made, n + 1)
                dve.reciprocal(rstd[:, n:n + 1], std[:, n:n + 1]).then_inc(rstd_made, 1)
                dve.wait_ge(rstd_made, n + 1)
                for k, made in enumerate((xn_a, xn_ready)):
                    dve.tensor_scalar(xn[:, half[k]], x[:, half[k]], meanvar[:, n, 0:1], rstd[:, n:n + 1],
                                      ALU.subtract, ALU.mult).then_inc(made, 1)
                dve.wait_ge(xnT_psum_a, n + 1)
                dve.tensor_copy(xnT[:, 0:2, :], ps_xT[0][:, 0:2 * P].rearrange("p (c t) -> p c t", c=2))\
                   .then_inc(xnT_a, 1)

            dve.wait_ge(x_in, 16)
            take_stats(0, 0)
            take_stats(0, 1)
            layer_norm(0)
            for a in range(2):
                def spread_k(m):
                    c = DC * a + m
                    if a == 0:
                        dve.wait_ge(k_psum, 1)
                        dve.wait_ge(const_made, 5)
                        src = ps_k[:, m * P:(m + 1) * P]
                    else:
                        dve.wait_ge(k_psum, m + 2)
                        src = ps_k[:, 0:P]
                    if c >= 2:
                        dve.wait_ge(s_psum, c - 1)
                    dve.tensor_tensor(kx[:, c % 2], src.unsqueeze(1).to_broadcast([P, HPC, P]),
                                      headmask[:, :].unsqueeze(2).to_broadcast([P, HPC, P]),
                                      ALU.mult).then_inc(k_ready, 1)

                def mask(m):
                    c = DC * a + m
                    dve.wait_ge(s_psum, c + 1)
                    if c >= DC:
                        dve.wait_ge(probT_psum, c - DC + 1)
                    dve.scalar_tensor_tensor(prob[:, m], ps_s[c % 2][:, :].rearrange("p (h k) -> p h k", h=HPC),
                                             SCALE, causal[:, :].unsqueeze(1).to_broadcast([P, HPC, P]),
                                             ALU.mult, ALU.add).then_inc(s_masked, 1)
                    dve.wait_ge(s_masked, c + 1)
                    dve.tensor_reduce(nmax[:, c], prob[:, m], AX_X, ALU.max, negate=True)\
                       .then_inc(nmax_ready, 1)

                def invert(m):
                    c = DC * a + m
                    dve.wait_ge(exp_done, c + 1)
                    dve.reciprocal(rrow[:, c], rowsum[:, c]).then_inc(rrow_ready, 1)
                    if m == DC - 1:
                        dve.wait_ge(rrow_ready, c + 1)
                        dve.tensor_tensor(prob[:, m], prob[:, m],
                                          rrow[:, c].unsqueeze(2).to_broadcast([P, HPC, P]),
                                          ALU.mult).then_inc(last_prob_ready, 1)

                def copy_o(m):
                    c = DC * a + m
                    dve.wait_ge(o_psum, c + 1)
                    dve.tensor_copy(oT[:, m, :], ps_o[:, m * P:(m + 1) * P]).then_inc(o_ready, 1)

                def copy_v():
                    dve.wait_ge(v_psum, a + 1)
                    dve.tensor_copy(v, ps_v[:, :]).then_inc(v_ready, 1)

                spread_k(0)
                spread_k(1)
                mask(0)
                if a == 0:
                    copy_v()
                spread_k(2)
                mask(1)
                invert(0)
                spread_k(3)
                mask(2)
                invert(1)
                mask(3)
                invert(2)
                if a == 1:
                    copy_v()
                invert(3)
                copy_o(0)
                copy_o(1)
                copy_o(2)
                copy_o(3)
                for k, out_half in enumerate((z_psum_a, z_psum)):
                    dve.wait_ge(out_half, a + 1)
                    dve.tensor_tensor(x[:, half[k]], ps_z[k][:, 0:D // 2], x[:, half[k]], ALU.add)\
                       .then_inc(x_ready, 1)
                    dve.wait_ge(x_ready, 2 * a + k + 1)
                    take_stats(a + 1, k)
                layer_norm(a + 1)

            step = [0]

            def then(ins):
                step[0] += 1
                ins.then_inc(route, 1)
                dve.wait_ge(route, step[0])

            dve.wait_ge(x_part[0], 1)
            dve.tensor_tensor(x_rest, xn[:, :], x_parts[:, 0, :], ALU.subtract).then_inc(x_rest_ready, 1)
            dve.wait_ge(x_part[1], 1)
            dve.tensor_tensor(x_parts[:, 2, :], x_rest, x_parts[:, 1, :], ALU.subtract).then_inc(x_part[2], 1)
            dve.wait_ge(gate_psum, 1)
            then(dve.tensor_reduce(lmax[:, :], ps_g[:, 0:E], AX_X, ALU.max, negate=True))
            dve.wait_ge(lexp_ready, 1)
            then(dve.reciprocal(rlsum[:, :], lsum[:, :]))
            then(dve.tensor_scalar(score[:, 0:E], lexp[:, :], rlsum[:, :], None, ALU.mult))
            then(dve.max(lexp[:, 0:8], score[:, 0:E]))
            then(dve.tensor_copy(top[:, 0:TOP_K], lexp[:, 0:TOP_K]))
            then(dve.match_replace(rest[:, :], top[:, :], score[:, :], -3.0))
            dve.tensor_scalar(chosen[:, :], rest[:, 0:E], 0.0, None, ALU.is_lt).then_inc(chosen_ready, 1)
            then(dve.tensor_reduce(wsum[:, :], top[:, 0:TOP_K], AX_X, ALU.add))
            then(dve.tensor_scalar(wsum[:, :], wsum[:, :], 1e-20, None, ALU.add))
            then(dve.reciprocal(rwsum[:, :], wsum[:, :]))
            then(dve.tensor_scalar(weight[:, :], score[:, 0:E], rwsum[:, :], None, ALU.mult))
            def column(t, e):
                return t[:, bass.ds(e, 1)]

            def make_gather(p):
                if not isinstance(p, int) or p >= 1:
                    dve.wait_ge(xe_psum_b, p)
                for e in range(2):
                    last = dve.tensor_scalar(gather[:, e * SLOTS:(e + 1) * SLOTS], slot_no[:, :],
                                             column(place, p * 2 + e), None, ALU.is_equal)
                last.then_inc(gather_ready, 1)

            def make_scatter(p):
                for e in range(2):
                    last = dve.tensor_scalar(scatter[:, e * SLOTS:(e + 1) * SLOTS], slot_no[:, :],
                                             column(place, p * 2 + e), column(weight, p * 2 + e),
                                             ALU.is_equal, ALU.mult)
                last.then_inc(scatter_ready, 1)

            def shared_h(half):
                dve.wait_ge(silu_ready, half + 1)
                dve.wait_ge(up_psum, half + 1)
                dve.tensor_tensor(h, ps_u[:, 0:F], silu, ALU.mult).then_inc(h_ready, 1)

            def read_slots(p):
                dve.wait_ge(scatter_psum, p + 1)
                dve.tensor_reduce(slot_w[:, :], ps_sc[:, 0:P], AX_X, ALU.add).then_inc(slot_w_ready, 1)

            def make_slots(p):
                if not isinstance(p, int) or p >= 1:
                    dve.wait_ge(y_psum, p)
                dve.tensor_scalar(slots[:, :], ps_sc[:, 0:P], 0.0, None, ALU.is_gt)\
                   .then_inc(slots_ready, 1)

            def pair_h(p):
                dve.wait_ge(silu_ready, p + 3)
                dve.wait_ge(slot_w_ready, p + 1)
                dve.wait_ge(up_psum, p + 3)
                dve.scalar_tensor_tensor(h, ps_u[:, 0:F], slot_w[:, :], silu, ALU.mult, ALU.mult)\
                   .then_inc(h_ready, 1)

            def copy_xe(p):
                dve.wait_ge(xe_psum_a, p + 1)
                dve.tensor_copy(xeT[:, 0:2, :], ps_xe[0][:, 0:2 * P].rearrange("p (c s) -> p c s", c=2))\
                   .then_inc(xe_a, 1)

            def split_ye(p):
                dve.wait_ge(ye_hi_ready, p + 1)
                dve.tensor_tensor(ye_lo[:, :], ps_ye[:, :], ye_hi[:, :].bitcast(F32), ALU.subtract)\
                   .then_inc(ye_ready, 1)

            shared_h(0)
            dve.wait_ge(chosen_ready, 1)
            dve.wait_ge(count_psum, 1)
            then(dve.scalar_tensor_tensor(place[:, :], ps_r[:, 0:E], 1.0, chosen[:, :], ALU.add, ALU.mult))
            make_gather(0)
            make_scatter(0)
            dve.wait_ge(hT_psum, 1)
            shared_h(1)
            copy_xe(0)

            def pair_step(p):
                make_gather(p + 1)
                read_slots(p)
                make_scatter(p + 1)
                pair_h(p)
                copy_xe(p + 1)
                make_slots(p)
                split_ye(p)

            pair_step(0)
            with dve.Fori(0, 2) as i:
                for j in range(RING):
                    pair_step(i * RING + (j + 1))
            for p in range(2 * RING + 1, PAIRS - 1):
                pair_step(p)
            read_slots(PAIRS - 1)
            pair_h(PAIRS - 1)
            make_slots(PAIRS - 1)
            split_ye(PAIRS - 1)
            dve.wait_ge(y_psum, PAIRS)
            dve.tensor_tensor(final, ps_y[:, :], x[:, :], ALU.add).then_inc(final_ready, 1)

        @block.tensor
        def _(pe):
            def stay_busy(n, out=ps_v):
                for _ in range(n):
                    pe.matmul(out[:, 0:P], ones[:, :], ones[:, :], start=True, stop=True)

            def transpose_xn(n):
                for k, (made, done) in enumerate(((xn_a, xnT_psum_a), (xn_ready, xnT_psum_b))):
                    pe.wait_ge(made, n + 1)
                    for c in (2 * k, 2 * k + 1):
                        last = pe.transpose(ps_xT[k][:, (c % 2) * P:(c % 2 + 1) * P],
                                            xn[:, c * P:(c + 1) * P], ident[:, :])
                    last.then_inc(done, 1)

            pe.wait_ge(ones_set, 1)
            stay_busy(36)
            pe.wait_ge(k_in, 32)
            for m in range(DC):
                last = pe.matmul(ps_k[:, m * P:(m + 1) * P], kv_w[:, m * P:(m + 1) * P], ctxT[:, :],
                                 start=True, stop=True)
            last.then_inc(k_psum, 1)
            pe.wait_ge(const_made, 5)
            transpose_xn(0)

            for a in range(2):
                stay_busy(8)
                pe.wait_ge(q_in[a], 16)
                pe.wait_ge(xnT_a, a + 1)

                def project(m):
                    c = DC * a + m
                    if m >= 1:
                        pe.wait_ge(q_ready, c)
                    for k in range(DC):
                        if m == 0 and k == 2:
                            pe.wait_ge(xnT_b, a + 1)
                        last = pe.matmul(ps_q[:, 0:P], q_w[a][:, k, m * P:(m + 1) * P], xnT[:, k, :],
                                         start=(k == 0), stop=(k == DC - 1))
                    last.then_inc(q_psum, 1)
                    if a == 1:
                        if m == 0:
                            pe.wait_ge(aw_in[1], 16)
                        pe.wait_ge(k_ready, c)
                        for k in range(DC):
                            last = pe.matmul(ps_k[:, 0:P], a_w[1][:, k, m * P:(m + 1) * P], xnT[:, k, :],
                                             start=(k == 0), stop=(k == DC - 1))
                        last.then_inc(k_psum, 1)

                def context_values():
                    pe.wait_ge(v_in, 16)
                    pe.matmul(ps_v[:, :], ctxT[:, :], kv_w[:, D:2 * D], start=True, stop=True)\
                      .then_inc(v_psum, 1)

                def values():
                    pe.wait_ge(aw_in[2], 16)
                    for k in range(DC):
                        last = pe.matmul(ps_v[:, :], xnT[:, k, :], a_w[2][:, k, :],
                                         start=(k == 0), stop=(k == DC - 1))
                    last.then_inc(v_psum, 1)

                def scores(m):
                    c = DC * a + m
                    pe.wait_ge(q_ready, c + 1)
                    pe.wait_ge(k_ready, c + 1)
                    if c >= 2:
                        pe.wait_ge(s_masked, c - 1)
                    pe.matmul(ps_s[c % 2][:, :], qT[:, m, :], kx[:, c % 2], start=True, stop=True)\
                      .then_inc(s_psum, 1)

                def transpose_prob(m):
                    c = DC * a + m
                    if m == DC - 1:
                        pe.wait_ge(last_prob_ready, a + 1)
                    else:
                        pe.wait_ge(prob_ready, (DC - 1) * a + m + 1)
                    if c >= 1:
                        pe.wait_ge(probT_ready, c)
                    for k in range(HPC):
                        last = pe.transpose(ps_t[:, k * P:(k + 1) * P], prob[:, m, k, :], ident[:, :])
                    last.then_inc(probT_psum, 1)

                def weighted_values(m):
                    c = DC * a + m
                    pe.wait_ge(probT_ready, c + 1)
                    pe.wait_ge(v_ready, a + 1)
                    if c >= 1:
                        pe.wait_ge(o_ready, c)
                    for k in range(HPC):
                        n = (m * HPC + k) * HD
                        last = pe.matmul(ps_o[k * HD:(k + 1) * HD, m * P:(m + 1) * P], v[:, n:n + HD],
                                         probT[:, c % 2, k, :], start=True, stop=True)
                    last.then_inc(o_psum, 1)

                def output(m):
                    c = DC * a + m
                    pe.wait_ge(o_ready, c + 1)
                    if m == 0:
                        pe.wait_ge(o_in[a], 16)
                        pe.wait_ge(s_masked, c + 3)
                    for k, done in enumerate((z_psum_a, z_psum)):
                        last = pe.matmul(ps_z[k][:, 0:D // 2], oT[:, m, :],
                                         o_w[a][:, m, k * (D // 2):(k + 1) * (D // 2)],
                                         start=(m == 0), stop=(m == DC - 1))
                        if m == DC - 1:
                            last.then_inc(done, 1)

                project(0)
                project(1)
                scores(0)
                if a == 0:
                    context_values()
                project(2)
                scores(1)
                project(3)
                scores(2)
                transpose_prob(0)
                scores(3)
                if a == 1:
                    values()
                weighted_values(0)
                transpose_prob(1)
                output(0)
                weighted_values(1)
                transpose_prob(2)
                output(1)
                weighted_values(2)
                transpose_prob(3)
                output(2)
                weighted_values(3)
                output(3)
                stay_busy(40)
                transpose_xn(a + 1)

            stay_busy(8)

            def shared_gate(half):
                w = shared_gate_w[half]
                if half == 0:
                    pe.wait_ge(gate_in[0], 16)
                    pe.wait_ge(xnT_a, LN)
                for k in range(DC):
                    if half == 0 and k == 2:
                        pe.wait_ge(xnT_b, LN)
                    last = pe.matmul(ps_g[:, 0:w.shape[2]], xnT[:, k, :], w[:, k, :],
                                     start=(k == 0), stop=(k == DC - 1))
                last.then_inc(gate_psum, 1)

            def shared_up(half):
                if half == 0:
                    pe.wait_ge(up_in[0], 16)
                for k in range(DC):
                    last = pe.matmul(ps_u[:, 0:F], xnT[:, k, :], up_w(0)[:, k, half, :],
                                     start=(k == 0), stop=(k == DC - 1))
                last.then_inc(up_psum, 1)

            def transpose_h():
                for c in range(2):
                    pe.transpose(ps_h[:, c * P:(c + 1) * P], h[:, c * P:(c + 1) * P], ident[:, :])
                return pe.transpose(ps_h[0:FT, 2 * P:3 * P], h[:, 2 * P:F], ident[:, :])

            def shared_down(half):
                pe.wait_ge(hT_ready, half + 1)
                if half == 0:
                    pe.wait_ge(down_in[0], 16)
                    pe.wait_ge(tail_in[0], 16)
                for c in range(2):
                    pe.matmul(ps_y[:, :], hT[:, c * P:(c + 1) * P], down_w(0)[:, c, half, :],
                              start=(half == 0 and c == 0), stop=False)
                pe.matmul(ps_y[:, :], hT[0:FT, 2 * P:3 * P], tail_w(0)[:, half, :],
                          start=False, stop=False).then_inc(down_done, 1)

            def gather_tokens(p):
                pe.wait_ge(gather_ready, p + 1)
                for c in range(DC):
                    out, cols = ps_xe[c // 2][:, (c % 2) * P:(c % 2 + 1) * P], slice(c * P, (c + 1) * P)
                    for n in range(3):
                        last = pe.matmul(out, x_parts[:, n, cols], gather[:, :], start=(n == 0), stop=(n == 2))
                    if c == 1:
                        last.then_inc(xe_psum_a, 1)
                last.then_inc(xe_psum_b, 1)

            def pair_in(k, w, out):
                for e in range(2):
                    rows = slice(e * SLOTS, (e + 1) * SLOTS)
                    last = pe.matmul(out[rows, 0:F], xeT[:, k, rows], w[:, k, e, :],
                                     start=(k == 0), stop=(k == DC - 1))
                return last

            def pair_gate_begin(p, s, use):
                pe.wait_ge(xe_a, p + 1)
                pe.wait_ge(gate_in[s], use * 16)
                pe.wait_ge(silu_ready, p + 2)
                pair_in(0, gate_w(s), ps_g)
                pair_in(1, gate_w(s), ps_g)

            def pair_gate_end(p, s):
                pe.wait_ge(xe_b, p + 1)
                pair_in(2, gate_w(s), ps_g)
                pair_in(3, gate_w(s), ps_g).then_inc(gate_psum, 1)

            def pair_up(p, s, use):
                pe.wait_ge(up_in[s], use * 16)
                pe.wait_ge(h_ready, p + 2)
                for k in range(DC):
                    last = pair_in(k, up_w(s), ps_u)
                last.then_inc(up_psum, 1)

            def transpose_scatter(p):
                pe.wait_ge(scatter_ready, p + 1)
                if not isinstance(p, int) or p >= 1:
                    pe.wait_ge(slots_ready, p)
                pe.transpose(ps_sc[:, 0:P], scatter, ident[:, :]).then_inc(scatter_psum, 1)

            def transpose_pair_h(p):
                pe.wait_ge(hT_ready, p + 2)
                pe.wait_ge(h_ready, p + 3)
                transpose_h().then_inc(hT_psum, 1)

            def pair_down(p, s, use):
                pe.wait_ge(hT_ready, p + 3)
                pe.wait_ge(down_in[s], use * 16)
                for c in range(2):
                    for e in range(2):
                        rows = slice(e * SLOTS, (e + 1) * SLOTS)
                        at = c * P + e * SLOTS
                        pe.matmul(ps_ye[rows, :], hT[:, at:at + SLOTS], down_w(s)[:, c, e, :],
                                  start=(c == 0), stop=False)
                pe.wait_ge(tail_in[s], use * 16)
                for e in range(2):
                    rows = slice(e * SLOTS, (e + 1) * SLOTS)
                    at = 2 * P + e * SLOTS
                    last = pe.matmul(ps_ye[rows, :], hT[0:FT, at:at + SLOTS], tail_w(s)[:, e, :],
                                     start=False, stop=True)
                last.then_inc(down_done, 1)

            def add_pair(p, last_pair):
                pe.wait_ge(ye_ready, p + 1)
                pe.matmul(ps_y[:, :], slots[:, :], ye_hi[:, :], start=False, stop=False)
                pe.matmul(ps_y[:, :], slots[:, :], ye_lo[:, :], start=False, stop=last_pair)\
                  .then_inc(y_psum, 1)

            shared_gate(0)
            shared_up(0)
            pe.wait_ge(silu_ready, 1)
            shared_gate(1)
            pe.wait_ge(chosen_ready, 1)
            pe.matmul(ps_r[:, 0:E], before[:, :], chosen[:, :], start=True, stop=True).then_inc(count_psum, 1)
            pe.wait_ge(h_ready, 1)
            transpose_h().then_inc(hT_psum, 1)
            shared_up(1)
            shared_down(0)
            pe.wait_ge(x_part[2], 1)
            gather_tokens(0)
            pe.wait_ge(h_ready, 2)
            transpose_h().then_inc(hT_psum, 1)
            pair_gate_begin(0, 1, 1)
            shared_down(1)
            pair_gate_end(0, 1)

            def pair_step(p, i, j, first=False):
                s, t = (j + 1) % RING, (j + 2) % RING
                transpose_scatter(p)
                pair_up(p, s, i + 1 + (j + 1) // RING)
                gather_tokens(p + 1)
                if not first:
                    add_pair(p - 1, False)
                transpose_pair_h(p)
                pair_gate_begin(p + 1, t, i + 1 + (j + 2) // RING)
                pair_down(p, s, i + 1 + (j + 1) // RING)
                pair_gate_end(p + 1, t)

            for j in range(RING):
                pair_step(j, 0, j, first=j == 0)
            with pe.Fori(1, 3) as i:
                for j in range(RING):
                    pair_step(i * RING + j, i, j)
            last = PAIRS - 1
            s, use = PAIRS % RING, PAIRS // RING + 1
            transpose_scatter(last)
            pair_up(last, s, use)
            add_pair(last - 1, False)
            transpose_pair_h(last)
            pair_down(last, s, use)
            add_pair(last, True)


def kernel(x, ctx_512, L0_xattn_Wq, L0_xattn_Wkv_expand, L0_xattn_Wout, L0_attn_Wq, L0_attn_Wk, L0_attn_Wv,
           L0_attn_Wo, L0_ffn_wg_router, L0_ffn_w_gate, L0_ffn_w_up, L0_ffn_w_down, L0_ffn_ws_gate,
           L0_ffn_ws_up, L0_ffn_ws_down):
    import numpy as np
    import concourse.bacc as bacc
    from concourse.bass_utils import run_bass_kernel_spmd

    def chunks(w):
        w = np.asarray(w)
        return w.reshape(-1, P, w.shape[-1]).transpose(1, 0, 2).reshape(P, -1)

    def expert_slots(gate, up, down):
        n = gate.shape[0]

        def w_in(w):
            return w.reshape(n, 2, DC, P, F).transpose(0, 3, 2, 1, 4).reshape(n, P, GATE)

        main = down[:, :, :2 * P].reshape(n, 2, 2, P, D).transpose(0, 3, 2, 1, 4).reshape(n, P, 4 * D)
        tail = down[:, :, 2 * P:].transpose(0, 2, 1, 3).reshape(n, FT, 2 * D)
        return np.concatenate([w_in(gate), w_in(up), main], axis=2), tail

    def halves(w):
        return np.asarray(w).reshape(1, D, 2, F).transpose(0, 2, 1, 3)

    pair, pair_tail = expert_slots(
        np.asarray(L0_ffn_w_gate).reshape(PAIRS, 2, D, F), np.asarray(L0_ffn_w_up).reshape(PAIRS, 2, D, F),
        np.asarray(L0_ffn_w_down).reshape(PAIRS, 2, F, D))
    shared, shared_tail = expert_slots(
        halves(L0_ffn_ws_gate), halves(L0_ffn_ws_up), np.asarray(L0_ffn_ws_down).reshape(1, 2, F, D))
    first, second = shared[0][:, :GATE].reshape(P, DC, 2, F).transpose(2, 0, 1, 3)
    router = chunks(np.asarray(L0_ffn_wg_router).T).reshape(P, DC, E)
    shared_with_router = np.concatenate([np.concatenate([router, first], axis=2).reshape(P, -1),
                                         second.reshape(P, -1), shared[0][:, GATE:]], axis=1)
    arrays = {
        "x_d": np.asarray(x)[0],
        "ctxT_d": np.asarray(ctx_512)[0, :P].T,
        "xw_d": np.concatenate([chunks(np.asarray(L0_xattn_Wq).T), np.asarray(L0_xattn_Wkv_expand).T,
                                chunks(np.asarray(L0_xattn_Wout).T)], axis=1),
        "aw_d": np.concatenate([chunks(np.asarray(w).T) for w in (L0_attn_Wq, L0_attn_Wk, L0_attn_Wv,
                                                                  L0_attn_Wo)], axis=1),
        "sh_d": shared_with_router, "sh_tail_d": shared_tail[0],
        "pair_d": pair, "pair_tail_d": pair_tail,
    }
    arrays = {name: np.ascontiguousarray(a) for name, a in arrays.items()}
    nc = bacc.Bacc("TRN2", target_bir_lowering=False, num_devices=1)
    args = [nc.dram_tensor(name, a.shape, mybir.dt.from_np(a.dtype), kind="ExternalInput").ap()
            for name, a in arrays.items()]
    args.append(nc.dram_tensor("out_d", [P, D], F32, kind="ExternalOutput").ap())
    perceiver_layer(nc, *args)
    r = run_bass_kernel_spmd(nc, [arrays], core_ids=[0])
    return np.asarray(r.results[0]["out_d"]).reshape(1, P, D)
```
